# Optimizing a Trainium2 kernel written in Bass

```python
import numpy as np
import jax
import jax.numpy as jnp

def _softmax(x, axis=-1):
    return jax.nn.softmax(x, axis=axis)

def _gelu(x):
    return jax.nn.gelu(x, approximate=True)

def _silu(x):
    return jax.nn.silu(x)

def _sigmoid(x):
    return jax.nn.sigmoid(x)

def _layernorm(x, axis=-1, eps=1e-05):
    m = jnp.mean(x, axis=axis, keepdims=True)
    v = jnp.var(x, axis=axis, keepdims=True)
    return (x - m) / jnp.sqrt(v + eps)

def _scatter_add(tgt, idx, src, axis=0):
    return tgt.at[idx].add(src)

def _segment_sum(src, seg, n):
    return jax.ops.segment_sum(src, seg, n)
kernel_name = 'mk_xattn_ffn_d1_seqx_r4_3297f5'

def setup_inputs(seed: int=0):
    np.random.seed(seed)
    _w = jnp.asarray

    def _rec_inputs():
        import jax
        import jax.numpy as jnp
        _rk = jax.random.key(seed)
        x = 7.22e-05 + 1 * jax.random.normal(jax.random.fold_in(_rk, 1), (32, 256, 256), jnp.float32)
        _lenS = 256 - jax.random.randint(jax.random.fold_in(_rk, 7), (32,), 0, max(1, 256 // 4) + 1, jnp.int32)
        _lenS2 = 77 - jax.random.randint(jax.random.fold_in(_rk, 8), (32,), 0, max(1, 77 // 4) + 1, jnp.int32)
        _ctx_1024P = jax.random.normal(jax.random.fold_in(_rk, 11), (32, 16, 256), jnp.float32)
        _ctx_1024c = jax.random.dirichlet(jax.random.fold_in(_rk, 511), 0.3 * jnp.ones((16,), jnp.float32), (32, 77))
        _ctx_1024t = jnp.einsum('bsk,bkd->bsd', _ctx_1024c, _ctx_1024P)
        _ctx_1024t = _ctx_1024t * jax.lax.rsqrt(jnp.mean(jnp.square(_ctx_1024t)) + 1e-12) * 0.953939
        ctx_1024 = 4.13588e-05 + 0.999923 * (_ctx_1024t + 0.3 * jax.random.normal(jax.random.fold_in(_rk, 611), (32, 77, 256), jnp.float32))
        return (x, ctx_1024)
    x, ctx_1024 = _rec_inputs()

    def _L0_xattn_setup():
        import jax, jax.numpy as jnp
        import numpy as np
        B, T, D, H = (4, 512, 256, 8)
        HD = D // H

        def _heads(t):
            b, t_, _ = t.shape
            return t.reshape(b, t_, H, HD).transpose(0, 2, 1, 3)
        key = jax.random.key(seed)
        ks = jax.random.split(key, 10)
        s = 1.0 / np.sqrt(D)
        return {'x': jax.random.normal(ks[0], (B, T, D), jnp.float32), 'y': jax.random.normal(ks[1], (B, T, D), jnp.float32), 'Wq': jax.random.normal(ks[2], (D, D), jnp.float32) * s, 'bq': jnp.zeros((D,), jnp.float32), 'Wk': jax.random.normal(ks[3], (D, D), jnp.float32) * s, 'bk': jnp.zeros((D,), jnp.float32), 'Wv': jax.random.normal(ks[4], (D, D), jnp.float32) * s, 'bv': jnp.zeros((D,), jnp.float32), 'Wo': jax.random.normal(ks[5], (D, D), jnp.float32) * s, 'bo': jnp.zeros((D,), jnp.float32)}
    _L0_xattn_all = _L0_xattn_setup()
    _L0_xattn_in = {k: v for k, v in _L0_xattn_all.items() if k in ('Wq', 'bq', 'Wk', 'bk', 'Wv', 'bv', 'Wo', 'bo')}
    del _L0_xattn_all

    def _L0_ffn_setup():
        import jax, jax.numpy as jnp
        import numpy as np
        D_IN, D_HID = (256, 1024)

        def _ternary(key, shape):
            return jax.random.randint(key, shape, -1, 2).astype(jnp.float32)

        def _tlin(x, w, s):
            return jnp.einsum('bsi,oi->bso', x, w) * s
        key = jax.random.key(seed)
        ks = jax.random.split(key, 12)
        inv = lambda fan: 1.0 / np.sqrt(fan).astype(np.float32)
        return {'x': jax.random.normal(ks[0], (4, 512, D_IN), dtype=jnp.float32), 'w1_w': _ternary(ks[1], (D_HID, D_IN)), 'w1_s': jax.random.uniform(ks[2], (D_HID,), dtype=jnp.float32) * inv(D_IN), 'w2_w': _ternary(ks[3], (D_HID, D_IN)), 'w2_s': jax.random.uniform(ks[4], (D_HID,), dtype=jnp.float32) * inv(D_IN), 'h1_w': _ternary(ks[5], (D_HID, D_HID)), 'h1_s': jax.random.uniform(ks[6], (D_HID,), dtype=jnp.float32) * inv(D_HID), 'h2_w': _ternary(ks[7], (D_HID, D_HID)), 'h2_s': jax.random.uniform(ks[8], (D_HID,), dtype=jnp.float32) * inv(D_HID), 'w3_w': _ternary(ks[9], (D_IN, D_HID)), 'w3_s': jax.random.uniform(ks[10], (D_IN,), dtype=jnp.float32) * inv(D_HID)}
    _L0_ffn_all = _L0_ffn_setup()
    _L0_ffn_in = {k: v for k, v in _L0_ffn_all.items() if k in ('w1_w', 'w1_s', 'w2_w', 'w2_s', 'h1_w', 'h1_s', 'h2_w', 'h2_s', 'w3_w', 'w3_s')}
    del _L0_ffn_all
    return {'x': x, 'ctx_1024': ctx_1024, 'L0_xattn_Wq': _L0_xattn_in['Wq'], 'L0_xattn_bq': _L0_xattn_in['bq'], 'L0_xattn_Wk': _L0_xattn_in['Wk'], 'L0_xattn_bk': _L0_xattn_in['bk'], 'L0_xattn_Wv': _L0_xattn_in['Wv'], 'L0_xattn_bv': _L0_xattn_in['bv'], 'L0_xattn_Wo': _L0_xattn_in['Wo'], 'L0_xattn_bo': _L0_xattn_in['bo'], 'L0_ffn_w1_w': _L0_ffn_in['w1_w'], 'L0_ffn_w1_s': _L0_ffn_in['w1_s'], 'L0_ffn_w2_w': _L0_ffn_in['w2_w'], 'L0_ffn_w2_s': _L0_ffn_in['w2_s'], 'L0_ffn_h1_w': _L0_ffn_in['h1_w'], 'L0_ffn_h1_s': _L0_ffn_in['h1_s'], 'L0_ffn_h2_w': _L0_ffn_in['h2_w'], 'L0_ffn_h2_s': _L0_ffn_in['h2_s'], 'L0_ffn_w3_w': _L0_ffn_in['w3_w'], 'L0_ffn_w3_s': _L0_ffn_in['w3_s']}

def reference(x, ctx_1024, L0_xattn_Wq, L0_xattn_bq, L0_xattn_Wk, L0_xattn_bk, L0_xattn_Wv, L0_xattn_bv, L0_xattn_Wo, L0_xattn_bo, L0_ffn_w1_w, L0_ffn_w1_s, L0_ffn_w2_w, L0_ffn_w2_s, L0_ffn_h1_w, L0_ffn_h1_s, L0_ffn_h2_w, L0_ffn_h2_s, L0_ffn_w3_w, L0_ffn_w3_s):
    import jax
    import jax.numpy as jnp

    def _L0_xattn_ref(x, y, Wq, bq, Wk, bk, Wv, bv, Wo, bo):
        import jax, jax.numpy as jnp
        import numpy as np
        B, T, D, H = (4, 512, 256, 8)
        HD = D // H

        def _heads(t):
            b, t_, _ = t.shape
            return t.reshape(b, t_, H, HD).transpose(0, 2, 1, 3)
        Tq, Tk = (x.shape[1], y.shape[1])
        q = _heads(x @ Wq.T + bq)
        k = _heads(y @ Wk.T + bk)
        v = _heads(y @ Wv.T + bv)
        scale = 1.0 / np.sqrt(HD)
        logits = jnp.einsum('bhqd,bhkd->bhqk', q, k) * scale
        causal = jnp.triu(jnp.full((Tq, Tk), -jnp.inf, jnp.float32), k=1)
        logits = logits + causal
        attn = jax.nn.softmax(logits, axis=-1)
        ctx = jnp.einsum('bhqk,bhkd->bhqd', attn, v)
        ctx = ctx.transpose(0, 2, 1, 3).reshape(x.shape[0], Tq, D)
        out = ctx @ Wo.T + bo
        return out

    def _L0_ffn_ref(x, w1_w, w1_s, w2_w, w2_s, h1_w, h1_s, h2_w, h2_s, w3_w, w3_s):
        import jax, jax.numpy as jnp
        import numpy as np
        D_IN, D_HID = (256, 1024)

        def _ternary(key, shape):
            return jax.random.randint(key, shape, -1, 2).astype(jnp.float32)

        def _tlin(x, w, s):
            return jnp.einsum('bsi,oi->bso', x, w) * s
        h = jax.nn.silu(_tlin(x, w1_w, w1_s)) * _tlin(x, w2_w, w2_s)
        h = jax.nn.gelu(_tlin(h, h1_w, h1_s), approximate=False)
        h = jax.nn.gelu(_tlin(h, h2_w, h2_s), approximate=False)
        return _tlin(h, w3_w, w3_s)
    x = x + _L0_xattn_ref(_layernorm(x, axis=-1), ctx_1024, L0_xattn_Wq, L0_xattn_bq, L0_xattn_Wk, L0_xattn_bk, L0_xattn_Wv, L0_xattn_bv, L0_xattn_Wo, L0_xattn_bo)
    x = x + _L0_ffn_ref(_layernorm(x, axis=-1), L0_ffn_w1_w, L0_ffn_w1_s, L0_ffn_w2_w, L0_ffn_w2_s, L0_ffn_h1_w, L0_ffn_h1_s, L0_ffn_h2_w, L0_ffn_h2_s, L0_ffn_w3_w, L0_ffn_w3_s)
    return x

_drawn_inputs = setup_inputs


def setup_inputs(seed=0):
    import zlib

    import numpy as np

    out = dict(_drawn_inputs(seed))
    spreads = {'L0_xattn_bq': (0.0, 0.1),
     'L0_xattn_bk': (0.0, 0.1),
     'L0_xattn_bv': (0.0, 0.1),
     'L0_xattn_bo': (0.0, 0.1)}
    factors = {}
    for name, (base, spread) in spreads.items():
        noise = np.random.default_rng([zlib.crc32(name.encode()), seed]).standard_normal(out[name].shape)
        drawn = base * np.exp(spread * noise) if base else spread * noise
        out[name] = jnp.asarray(drawn.astype(out[name].dtype))
    for name, factor in factors.items():
        out[name] = (out[name] * factor).astype(out[name].dtype)
    return out
```

```python
from contextlib import ExitStack

import concourse.bass as bass
from concourse import mybir

F32 = mybir.dt.float32
F32R = mybir.dt.float32r
I32 = mybir.dt.int32
ALU = mybir.AluOpType
ACT = mybir.ActivationFunctionType
AX_X = mybir.AxisListType.X

P = 128
B, TQ, TK, D = 32, 256, 77, 256
H = 8
HD = D // H
HID = 1024
TILE = 512
NB = TILE // TQ
NT = B // NB
NQ = TILE // P
KD = D // P
KH = HID // P
HG = H // 4
G4 = 4 * TK
SCALE = float(HD) ** -0.5
EPS = 1e-5
MASKED = -3.0e38
CHUNK = 2048
STAGES = 7

ORDER = [
    ("L1", 0), ("T1", 0), ("L1", 1), ("KV", 0), ("L1", 2), ("Q", 0), ("L1", 3), ("S", 0),
    ("L1", 4), ("S", 1), ("L1", 5), ("S", 2), ("L1", 6), ("L1", 7), ("L1E", 0), ("S", 3),
    ("EXP", 0), ("EXP", 1), ("EXP", 2), ("EXP", 3),
    ("L2", 0), ("L2", 1), ("L2", 2), ("PT", 0), ("L2", 3), ("PT", 1), ("L2", 4), ("PV", 0),
    ("PT", 2), ("L2", 5), ("PT", 3), ("L2", 6), ("PV", 1), ("SEED", 0), ("L2", 7),
    ("L3", 0), ("O", 0), ("L3", 1), ("L3", 2), ("LN2S", 0), ("L3", 3), ("L3", 4), ("LN2A", 0),
    ("L3", 5), ("LN1S", 0), ("L3", 6), ("L3", 7), ("T2", 0), ("CTX", 0), ("L4", 0), ("LN1A", 0),
    ("L4", 1),
]
FFN = ("L1", "L1E", "L2", "L3", "L4")
NEXT = ("LN1S", "LN1A", "CTX")


def steps(ffn, att, nxt):
    return [(s, n) for s, n in ORDER if (ffn if s in FFN else nxt if s in NEXT else att)]


FIRST = [
    ("KV", 0), ("T1", 0), ("ROUND", 0), ("Q", 0), ("CHECK", 0), ("ROUND", 1), ("CHECK", 1), ("ROUND", 2),
    ("S", 0), ("S", 1), ("S", 2), ("S", 3), ("EXP", 0), ("ROUND", 3), ("EXP", 1), ("EXP", 2),
    ("EXP", 3), ("ROUND", 4), ("ROUND", 5), ("CHECK", 2), ("PT", 0), ("PT", 1), ("CHECK", 3), ("PV", 0),
    ("ROUND", 6), ("PT", 2), ("CHECK", 4), ("PT", 3), ("CHECK", 5), ("PV", 1), ("SEED", 0), ("ROUND", 7),
    ("CHECK", 6), ("CHECK", 7), ("O", 0), ("ROUND", 8), ("ROUND", 9), ("LN2S", 0), ("CHECK", 8), ("LN2A", 0),
    ("ROUND", 10), ("CHECK", 9), ("CHECK", 10), ("COUNT", 0), ("T2", 0), ("LN1S", 0), ("LN1A", 0), ("CTX", 0),
]


def build_kernel(nc, x, ctx_t, w_att, vectors, w1, w2, h1, h2, w3, out):
    x_tiles = x.rearrange("(t j p) d -> t p j d", j=NQ, p=P)
    out_tiles = out.rearrange("(t j p) d -> t p j d", j=NQ, p=P)
    ctx_tiles = ctx_t.rearrange("t p k c -> t p (k c)")

    with ExitStack() as es:
        def sem(name):
            return es.enter_context(nc.semaphore(name))

        slab_bytes = 211936
        es.enter_context(nc.sbuf_tensor("slab", [P, slab_bytes // 4], F32))
        base = nc.sbuf_base - slab_bytes
        top = [base]

        def put(name, shape, dt=F32, at=None):
            n = 4
            for s in shape[1:]:
                n *= s
            if at is None:
                at = top[0]
                top[0] += (n + 31) // 32 * 32
                assert top[0] <= base + slab_bytes, (name, top[0] - base)
            return nc.alloc_sbuf_tensor_at(name, shape, dt, offset=at), at

        w1_sb, _ = put("w1_sb", [P, KD, HID], F32R)
        w2_sb, _ = put("w2_sb", [P, KD, HID], F32R)
        h1_sb, _ = put("h1_sb", [P, KH, HID], F32R)
        h2_sb, _ = put("h2_sb", [P, KH, HID], F32R)
        w3_sb, _ = put("w3_sb", [P, KH, D], F32R)
        a_hi, a_hi_at = put("a_hi", [P, KH, TILE], F32R)
        a_lo, a_lo_at = put("a_lo", [P, KH, TILE], F32R)
        b_hi, b_hi_at = put("b_hi", [P, KH, TILE], F32R)
        b_lo, b_lo_at = put("b_lo", [P, KH, TILE], F32R)
        a_f32, _ = put("a_f32", [P, KH, TILE], at=a_lo_at)
        b_f32, _ = put("b_f32", [P, KH, TILE], at=b_lo_at)
        ln1_t, _ = put("ln1_t", [P, KD, TILE], at=b_lo_at)
        q_t, _ = put("q_t", [P, HG, TILE], at=b_lo_at + 4096)
        ctx_sb, _ = put("ctx_sb", [P, KD, NB * TK], at=b_lo_at + 8192)
        stage = [put(f"stage{i}", [P, CHUNK], at=[a_hi_at, a_lo_at, b_hi_at][i // 2] + 8192 * (i % 2))[0]
                 for i in range(STAGES - 1)]
        ln2_hi, ln2_at = put("ln2_hi", [P, KD, TILE], F32R)
        ln2_lo, _ = put("ln2_lo", [P, KD, TILE], F32R)
        attn_t, _ = put("attn_t", [TK, H, TQ], at=ln2_at)
        w_att_sb, _ = put("w_att_sb", [P, 4, KD, D])
        wq_sb, wk_sb, wv_sb, wo_sb = (w_att_sb[:, i] for i in range(4))
        x_in, _ = put("x_in", [P, NQ, D])
        xln, _ = put("xln", [P, NQ, D])
        x1_keep, keep_at = put("x1_keep", [P, NQ, D])
        out_sb, _ = put("out_sb", [P, NQ, D])
        stage.append(put("stage6", [P, CHUNK], at=keep_at)[0])
        k_diag, _ = put("k_diag", [P, HG, NB, G4])
        v_sb, _ = put("v_sb", [TK, NB, D])
        probs, probs_at = put("probs", [P, NQ, H * TK])
        heads_t, _ = put("heads_t", [P, KD, TILE], at=probs_at)
        x1, _ = put("x1", [P, NQ, D], at=probs_at + 2 * H * TK * 4)
        ring = [put(f"ring{i}", [P, P])[0] for i in range(2)]
        id32, _ = put("id32", [P, P])
        mask, _ = put("mask", [P, TK])
        n_small = 4 * KH + 2 * KD
        vec, _ = put("vec", [P, n_small + 3 * D])
        s1_sb, s2_sb, h1s_sb, h2s_sb = (vec[:, KH * i:KH * (i + 1)] for i in range(4))
        bq_sb, bk_sb = (vec[:, 4 * KH + KD * i:4 * KH + KD * (i + 1)] for i in range(2))
        bo_sb, bv_sb, s3_sb = (vec[:, n_small + D * i:n_small + D * (i + 1)] for i in range(3))
        mx, _ = put("mx", [P, NQ, H])
        total, _ = put("total", [P, NQ, H])
        rtotal, _ = put("rtotal", [P, NQ, H])
        st = [put(f"st{i}", [P, NQ, 6])[0] for i in range(2)]
        mv = [put(f"mv{i}", [P, NQ, 2])[0] for i in range(2)]
        veps = [put(f"veps{i}", [P, NQ])[0] for i in range(2)]
        rstd = [put(f"rstd{i}", [P, NQ])[0] for i in range(2)]
        spare, _ = put("spare", [P, 1])
        eps, _ = put("eps", [P, NQ])
        minus_half, _ = put("minus_half", [P, NQ])
        inexact, _ = put("inexact", [P, 11])
        inexact_row, _ = put("inexact_row", [P, 1])
        ones, _ = put("ones", [P, 1])
        flag, _ = put("flag", [1, 1], I32)

        fb = es.enter_context(nc.psum_tensor("ffn_banks", [P, 4, 512], F32))
        ab = es.enter_context(nc.psum_tensor("att_banks", [P, 4, 512], F32))

        x_loaded, ctx_loaded, stored = sem("x_loaded"), sem("ctx_loaded"), sem("stored")
        att_w_loaded, vec_loaded = sem("att_w_loaded"), sem("vec_loaded")
        staged = [sem(f"staged{i}") for i in range(STAGES)]
        ring_loaded = [sem("ring_loaded0"), sem("ring_loaded1")]
        ring_used = sem("ring_used")
        const_set, id_ready, kdiag_zero = sem("const_set"), sem("id_ready"), sem("kdiag_zero")
        dve_consts = sem("dve_consts")
        rounded, checked, row_summed = sem("rounded"), sem("checked"), sem("row_summed")
        flag_summed, flag_ready = sem("flag_summed"), sem("flag_ready")
        ln_stats = [sem("ln1_stats"), sem("ln2_stats")]
        ln_mv = [sem("ln1_mv"), sem("ln2_mv")]
        ln_veps = [sem("ln1_veps"), sem("ln2_veps")]
        ln_rstd = [sem("ln1_rstd"), sem("ln2_rstd")]
        ln_ready = [sem("ln1_ready"), sem("ln2_ready")]
        t1_ready, ln1t_done, k_ready, v_ready = sem("t1_ready"), sem("ln1t_done"), sem("k_ready"), sem("v_ready")
        k_done, v_done, q_ready, q_done = sem("k_done"), sem("v_done"), sem("q_ready"), sem("q_done")
        masked, s_ready, max_done, shifted, exp_done = sem("masked"), sem("s_ready"), sem("max_done"), sem("shifted"), sem("exp_done")
        sum_done, rsum_done, probs_ready = sem("sum_done"), sem("rsum_done"), sem("probs_ready")
        pt_ready, pt_act_done, pt_dve_done = sem("pt_ready"), sem("pt_act_done"), sem("pt_dve_done")
        pv_ready, heads_done, o_ready = sem("pv_ready"), sem("heads_done"), sem("o_ready")
        x1_seeded, x1_done, x1_kept = sem("x1_seeded"), sem("x1_done"), sem("x1_kept")
        t2_ready, ln2hi_done, ln2t_done = sem("t2_ready"), sem("ln2hi_done"), sem("ln2t_done")
        gate_ready, up_ready, silu_done, up_used = sem("gate_ready"), sem("up_ready"), sem("silu_done"), sem("up_used")
        h1_hi_done, h1_done = sem("h1_hi_done"), sem("h1_done")
        l2_ready, gelu2_done, h2_done = sem("l2_ready"), sem("gelu2_done"), sem("h2_done")
        l3_ready, gelu3_done, h3_done = sem("l3_ready"), sem("gelu3_done"), sem("h3_done")
        l4_ready, out_scaled, out_ready = sem("l4_ready"), sem("out_scaled"), sem("out_ready")

        pieces = []
        for dram, kept, cols in ((w1, w1_sb, HID), (w2, w2_sb, HID), (h1, h1_sb, HID), (h2, h2_sb, HID), (w3, w3_sb, D)):
            k_piece = CHUNK // cols
            for k in range(0, dram.shape[1], k_piece):
                pieces.append((dram[:, k:k + k_piece].rearrange("p k n -> p (k n)"),
                               kept[:, k:k + k_piece].rearrange("p k n -> p (k n)")))
        NP = len(pieces)

        def general_chunks(step, n):
            if step == "L1":
                return [w[:, k, n * P:(n + 1) * P] for w in (w1, w2) for k in range(KD)]
            if step in ("L2", "L3"):
                w = h1 if step == "L2" else h2
                return [w[:, k, n * P:(n + 1) * P] for k in range(KH)]
            if step == "L4":
                return [w3[:, k, c * P:(c + 1) * P] for _ in range(2) for c in range(KD) for k in range(KH)]
            return []

        CHUNKS = sum(len(general_chunks(s, n)) for s, n in ORDER if s in FFN)
        chunk_base = {}
        at = 0
        for s, n in ORDER:
            if s in FFN:
                chunk_base[s, n] = at
                at += len(general_chunks(s, n))

        block = es.enter_context(nc.Block())

        def whole_program(eng, one_pass):
            with eng.Fori(0, NT - 2) as f:
                one_pass(f, f + 1, True)
            one_pass(NT - 2, NT - 1, False)
            one_pass(NT - 1, None, False)

        @block.sync
        def _(sp):
            def load_x(t):
                src = x_tiles[t] if isinstance(t, int) else x_tiles[bass.ds(t, 1)].rearrange("a p j d -> (a p) j d")
                sp.dma_start(x_in[:], src).then_inc(x_loaded, 16)

            def load_ctx(t):
                src = ctx_tiles[t] if isinstance(t, int) else ctx_tiles[bass.ds(t, 1)].rearrange("a p c -> (a p) c")
                sp.dma_start(ctx_sb[:].rearrange("p k c -> p (k c)"), src).then_inc(ctx_loaded, 16)

            def load_piece(c):
                if c >= STAGES:
                    sp.wait_ge(checked, c - STAGES + 1)
                sp.dma_start(stage[c % STAGES][:], pieces[c][0]).then_inc(staged[c % STAGES], 16)

            def one_pass(f, a, nxt, general):
                for step, n in steps(True, a is not None, nxt) if f is not None else FIRST:
                    if step in FFN and general:
                        for i, src in enumerate(general_chunks(step, n)):
                            c = chunk_base[step, n] + i
                            sp.wait_ge(ring_used, CHUNKS * f + c + 1)
                            sp.dma_start(ring[c % 2][:], src).then_inc(ring_loaded[c % 2], 16)
                    if step == "CHECK" and n + STAGES < NP:
                        load_piece(n + STAGES)
                    if step == "SEED" and nxt:
                        sp.wait_ge(x1_seeded, a + 1)
                        load_x(a + 1)
                    if step == "CTX":
                        if f is None:
                            sp.wait_ge(v_ready, a + 1)
                        else:
                            sp.wait_ge(l3_ready, KH * f + KH)
                        load_ctx(a + 1)
                    if step == "L4" and n == 1:
                        sp.wait_ge(out_ready, 2 * f + 4)
                        dst = out_tiles[f] if isinstance(f, int) else out_tiles[bass.ds(f, 1)].rearrange("a p j d -> (a p) j d")
                        sp.dma_start(dst, out_sb[:]).then_inc(stored, 16)

            load_x(0)
            load_ctx(0)
            sp.dma_start(w_att_sb[:], w_att).then_inc(att_w_loaded, 16)
            sp.dma_start(vec[:], vectors).then_inc(vec_loaded, 16)
            for c in range(STAGES):
                load_piece(c)
            one_pass(None, 0, True, False)
            sp.wait_ge(flag_ready, 1)
            count = sp.value_load(flag[0:1, 0:1], min_val=0, max_val=1 << 23)
            with sp.If(count > 0):
                whole_program(sp, lambda f, a, nxt: one_pass(f, a, nxt, True))
            with sp.Else():
                whole_program(sp, lambda f, a, nxt: one_pass(f, a, nxt, False))
            sp.wait_ge(stored, 16 * (NT + 1))

        @block.tensor
        def _(pe):
            def product(psum, w_sb, rows, hi, lo, ready, base_n, w_is_moving=False):
                for k in range(rows):
                    if ready is not None:
                        pe.wait_ge(ready, base_n + k + 1)
                    for part, x_ap in enumerate((hi(k), lo(k))):
                        left, right = (x_ap, w_sb(k)) if w_is_moving else (w_sb(k), x_ap)
                        mm = nc.tensor.matmul(psum, left, right, start=(k == 0 and part == 0),
                                              stop=(k == rows - 1 and part == 1))
                return mm

            def product_general(psum, c, f, rows, hi, lo, ready, base_n, w_is_moving=False):
                for k in range(rows):
                    if ready is not None:
                        pe.wait_ge(ready, base_n + k + 1)
                    pe.wait_ge(ring_loaded[(c + k) % 2], (16 * (CHUNKS // 2)) * f + 16 * ((c + k) // 2 + 1))
                    for part, x_ap in enumerate((hi(k).bitcast(F32), lo(k).bitcast(F32))):
                        w_ap = ring[(c + k) % 2][:]
                        left, right = (x_ap, w_ap) if w_is_moving else (w_ap, x_ap)
                        mm = nc.tensor.matmul(psum, left, right, start=(k == 0 and part == 0),
                                              stop=(k == rows - 1 and part == 1))
                    mm.then_inc(ring_used, 1)
                return mm

            def signal(sem_, general):
                if general:
                    nc.tensor.drain().then_inc(sem_, 1)

            def one_pass(f, a, nxt, general):
                for step, n in steps(True, a is not None, nxt) if f is not None else FIRST:
                    c0 = chunk_base.get((step, n))
                    if step == "L1":
                        if n == 0:
                            pe.wait_ge(ln2t_done, f + 1)
                        if n == 1:
                            pe.wait_ge(out_scaled, 2 * f + 2)
                        for i, (w_sb, used, ready) in enumerate(((w1_sb, silu_done, gate_ready), (w2_sb, up_used, up_ready))):
                            if n >= 2:
                                pe.wait_ge(used, KH * f + n - 1)
                            bank = fb[:, 2 * (n % 2) + i, :]
                            hi, lo = (lambda k: ln2_hi[:, k, :]), (lambda k: ln2_lo[:, k, :])
                            if general:
                                product_general(bank, c0 + KD * i, f, KD, hi, lo, None, 0)
                                signal(ready, general)
                            else:
                                product(bank, lambda k: w_sb[:, k, n * P:(n + 1) * P], KD, hi, lo, None, 0).then_inc(ready, 1)
                    if step in ("L2", "L3"):
                        w_sb, src_hi, src_lo, h_done, ready, own = (
                            (h1_sb, a_hi, a_lo, h1_done, l2_ready, gelu2_done) if step == "L2"
                            else (h2_sb, b_hi, b_lo, h2_done, l3_ready, gelu3_done))
                        if n == 0 and step == "L2":
                            pe.wait_ge(silu_done, KH * f + KH - 1)
                        if n == 0 and step == "L3":
                            pe.wait_ge(gelu2_done, KH * f + KH - 3)
                        if n >= 4:
                            pe.wait_ge(own, KH * f + n - 3)
                        hi, lo = (lambda k: src_hi[:, k, :]), (lambda k: src_lo[:, k, :])
                        wait_h = h_done if n == 0 else None
                        bank = fb[:, n % 4, :]
                        if general:
                            product_general(bank, c0, f, KH, hi, lo, wait_h, KH * f)
                            signal(ready, general)
                        else:
                            product(bank, lambda k: w_sb[:, k, n * P:(n + 1) * P], KH, hi, lo, wait_h, KH * f).then_inc(ready, 1)
                    if step == "L4":
                        if n == 0:
                            pe.wait_ge(gelu3_done, KH * f + KH - 1)
                        for i in range(2):
                            j = 2 * n + i
                            hi, lo = (lambda k: a_hi[:, k, j * P:(j + 1) * P]), (lambda k: a_lo[:, k, j * P:(j + 1) * P])
                            wait_h = h3_done if j == 0 else None
                            if general:
                                for h in range(KD):
                                    product_general(fb[:, 2 + n, i * D + h * P:i * D + (h + 1) * P], c0 + (KD * i + h) * KH,
                                                    f, KH, hi, lo, wait_h if h == 0 else None, KH * f, w_is_moving=True)
                            else:
                                mm = product(fb[:, 2 + n, i * D:(i + 1) * D], lambda k: w3_sb[:, k, :], KH, hi, lo,
                                             wait_h, KH * f, w_is_moving=True)
                        if general:
                            signal(l4_ready, general)
                        else:
                            mm.then_inc(l4_ready, 1)
                    if step == "T1":
                        pe.wait_ge(ln_ready[0], a + 1)
                        for k in range(KD):
                            for j in range(NQ):
                                mm = nc.tensor.transpose(ab[:, k, j * P:(j + 1) * P], xln[:, j, k * P:(k + 1) * P], id32[:])
                        mm.then_inc(t1_ready, 1)
                    if step == "KV":
                        pe.wait_ge(ctx_loaded, 16 * (a + 1))
                        for m in range(HG):
                            for k in range(KD):
                                mm = nc.tensor.matmul(ab[:, 2, m * NB * TK:(m + 1) * NB * TK], wk_sb[:, k, m * P:(m + 1) * P],
                                                      ctx_sb[:, k, :], start=(k == 0), stop=(k == KD - 1))
                        mm.then_inc(k_ready, 1)
                        for b in range(NB):
                            for k in range(KD):
                                mm = nc.tensor.matmul(ab[0:TK, 3, b * D:(b + 1) * D], ctx_sb[:, k, b * TK:(b + 1) * TK],
                                                      wv_sb[:, k, :], start=(k == 0), stop=(k == KD - 1))
                        mm.then_inc(v_ready, 1)
                    if step == "Q":
                        pe.wait_ge(ln1t_done, a + 1)
                        for m in range(HG):
                            for k in range(KD):
                                mm = nc.tensor.matmul(ab[:, m, :], wq_sb[:, k, m * P:(m + 1) * P], ln1_t[:, k, :],
                                                      start=(k == 0), stop=(k == KD - 1))
                        mm.then_inc(q_ready, 1)
                    if step == "S":
                        if n == 0:
                            pe.wait_ge(q_done, a + 1)
                            pe.wait_ge(k_done, a + 1)
                            pe.wait_ge(v_done, a + 1)
                        if n >= 2:
                            pe.wait_ge(shifted, NQ * a + n - 1)
                        pair = 2 if n % 2 == 0 else 0
                        for g in range(HG):
                            mm = nc.tensor.matmul(ab[:, pair + g, 0:G4], q_t[:, g, n * P:(n + 1) * P],
                                                  k_diag[:, g, n // (TQ // P), :], start=True, stop=True)
                        mm.then_inc(s_ready, 1)
                    if step == "PT":
                        pe.wait_ge(probs_ready, NQ * a + n + 1)
                        if n < 2:
                            pe.wait_ge(shifted, NQ * a + n + 3)
                        if n == 3:
                            pe.wait_ge(heads_done, NB * a + 1)
                        pair = (2, 0, 0, 2)[n]
                        for h in range(H):
                            mm = nc.tensor.transpose(ab[0:TK, pair + h // 4, (h % 4) * P:(h % 4 + 1) * P],
                                                     probs[:, n, h * TK:(h + 1) * TK], id32[:])
                        mm.then_inc(pt_ready, 1)
                    if step == "PV":
                        pe.wait_ge(pt_act_done, NQ * a + 2 * n + 2)
                        pe.wait_ge(pt_dve_done, NQ * a + 2 * n + 2)
                        bank = (2, 0)[n]
                        for g in range(HG):
                            for h in range(4):
                                mm = nc.tensor.matmul(ab[HD * h:HD * (h + 1), bank, g * TQ:(g + 1) * TQ],
                                                      v_sb[:, n, (4 * g + h) * HD:(4 * g + h + 1) * HD],
                                                      attn_t[:, 4 * g + h, :], start=True, stop=True)
                        mm.then_inc(pv_ready, 1)
                    if step == "O":
                        pe.wait_ge(heads_done, NB * a + NB)
                        for j in range(NQ):
                            for k in range(KD):
                                mm = nc.tensor.matmul(ab[:, 2 + j // 2, (j % 2) * D:(j % 2 + 1) * D],
                                                      heads_t[:, k, j * P:(j + 1) * P], wo_sb[:, k, :],
                                                      start=(k == 0), stop=(k == KD - 1))
                        mm.then_inc(o_ready, 1)
                    if step == "T2":
                        pe.wait_ge(ln_ready[1], a + 1)
                        for k in range(KD):
                            for j in range(NQ):
                                mm = nc.tensor.transpose(ab[:, k, j * P:(j + 1) * P], xln[:, j, k * P:(k + 1) * P], id32[:])
                        mm.then_inc(t2_ready, 1)

            pe.wait_ge(id_ready, 1)
            pe.wait_ge(att_w_loaded, 16)
            pe.wait_ge(kdiag_zero, 1)
            one_pass(None, 0, True, False)
            pe.wait_ge(row_summed, 1)
            nc.tensor.matmul(fb[0:1, 0, 0:1], inexact_row[:], ones[:], start=True, stop=True).then_inc(flag_summed, 1)
            pe.wait_ge(flag_ready, 1)
            count = pe.value_load(flag[0:1, 0:1], min_val=0, max_val=1 << 23)
            with pe.If(count > 0):
                whole_program(pe, lambda f, a, nxt: one_pass(f, a, nxt, True))
            with pe.Else():
                whole_program(pe, lambda f, a, nxt: one_pass(f, a, nxt, False))

        @block.scalar
        def _(act):
            def one_pass(f, a, nxt):
                for step, n in steps(True, a is not None, nxt) if f is not None else FIRST:
                    if step == "ROUND":
                        act.wait_ge(staged[n % STAGES], 16 * (n // STAGES + 1))
                        nc.scalar.copy(pieces[n][1], stage[n % STAGES][:]).then_inc(rounded, 1)
                    if step == "L1":
                        act.wait_ge(gate_ready, KH * f + n + 1)
                        nc.scalar.activation(a_f32[:, n, :], fb[:, 2 * (n % 2), :], ACT.Silu,
                                             scale=s1_sb[:, n:n + 1]).then_inc(silu_done, 1)
                    if step == "L1" and n == 0:
                        act.wait_ge(x1_done, f + 1)
                        act.wait_ge(out_ready, 2 * f + 2)
                        nc.scalar.copy(x1_keep[:], x1[:]).then_inc(x1_kept, 1)
                    if (step == "L1" and n > 0) or step == "L1E":
                        m = n - 1 if step == "L1" else KH - 1
                        act.wait_ge(up_used, KH * f + m + 1)
                        nc.scalar.copy(a_hi[:, m, :], a_f32[:, m, :]).then_inc(h1_hi_done, 1)
                    if step in ("L2", "L3"):
                        f32, hi, scale, ready, done = ((b_f32, b_hi, h1s_sb, l2_ready, gelu2_done) if step == "L2"
                                                       else (a_f32, a_hi, h2s_sb, l3_ready, gelu3_done))
                        act.wait_ge(ready, KH * f + n + 1)
                        nc.scalar.activation(f32[:, n, :], fb[:, n % 4, :], ACT.Gelu, scale=scale[:, n:n + 1])
                        nc.scalar.activation(hi[:, n, :], fb[:, n % 4, :], ACT.Gelu, scale=scale[:, n:n + 1]).then_inc(done, 1)
                    if step == "T1":
                        act.wait_ge(t1_ready, a + 1)
                        nc.scalar.copy(ln1_t[:], ab[:, 0:2, :]).then_inc(ln1t_done, 1)
                    if step == "KV":
                        act.wait_ge(k_ready, a + 1)
                        for g in range(HG):
                            for h in range(4):
                                rows = slice(HD * h, HD * (h + 1))
                                op = nc.scalar.activation(
                                    k_diag[rows, g, :, h * TK:(h + 1) * TK],
                                    ab[rows, 2, g * NB * TK:(g + 1) * NB * TK].rearrange("p (b c) -> p b c", b=NB),
                                    ACT.Identity, bias=bk_sb[rows, g:g + 1])
                        op.then_inc(k_done, 1)
                    if step == "Q":
                        act.wait_ge(q_ready, a + 1)
                        for g in range(HG):
                            op = nc.scalar.activation(q_t[:, g, :], ab[:, g, :], ACT.Identity, bias=bq_sb[:, g:g + 1])
                        op.then_inc(q_done, 1)
                    if step == "EXP":
                        act.wait_ge(shifted, NQ * a + n + 1)
                        nc.scalar.activation(probs[:, n, :], probs[:, n, :], ACT.Exp, scale=SCALE).then_inc(exp_done, 1)
                    if step == "PT":
                        act.wait_ge(pt_ready, NQ * a + n + 1)
                        q0 = (n % 2) * P
                        nc.scalar.copy(attn_t[:, 0:4, q0:q0 + P],
                                       ab[0:TK, (2, 0, 0, 2)[n], :].rearrange("p (h q) -> p h q", h=4)).then_inc(pt_act_done, 1)
                    if step == "PV":
                        act.wait_ge(pv_ready, NB * a + n + 1)
                        nc.scalar.copy(heads_t[:, :, n * TQ:(n + 1) * TQ],
                                       ab[:, (2, 0)[n], :].rearrange("p (g q) -> p g q", g=HG)).then_inc(heads_done, 1)
                    if step == "T2":
                        act.wait_ge(t2_ready, a + 1)
                        nc.scalar.copy(ln2_hi[:], ab[:, 0:2, :]).then_inc(ln2hi_done, 1)

            act.wait_ge(vec_loaded, 16)
            act.wait_ge(kdiag_zero, 1)
            one_pass(None, 0, True)
            whole_program(act, one_pass)

        @block.vector
        def _(dve):
            def ln_stats_of(src, i, a):
                for j in range(NQ):
                    op = nc.vector.bn_stats(st[i][:, j, :], src[:, j, :])
                op.then_inc(ln_stats[i], 1)
                dve.wait_ge(ln_stats[i], a + 1)
                nc.vector.memset(spare[:], 0.0)
                for j in range(NQ):
                    op = nc.vector.bn_aggr(mv[i][:, j, :], st[i][:, j, :])
                op.then_inc(ln_mv[i], 1)

            def ln_apply(src, i, a):
                dve.wait_ge(ln_rstd[i], a + 1)
                for j in range(NQ):
                    op = nc.vector.tensor_scalar(xln[:, j, :], src[:, j, :], mv[i][:, j, 0:1], rstd[i][:, j:j + 1],
                                                 ALU.subtract, ALU.mult)
                op.then_inc(ln_ready[i], 1)

            def soften(n, a):
                p = probs[:, n, :].rearrange("p (h c) -> p h c", h=H)
                dve.wait_ge(exp_done, NQ * a + n + 1)
                nc.vector.tensor_reduce(total[:, n, :], p, AX_X, ALU.add).then_inc(sum_done, 1)
                dve.wait_ge(sum_done, NQ * a + n + 1)
                nc.vector.reciprocal(rtotal[:, n, :], total[:, n, :]).then_inc(rsum_done, 1)
                dve.wait_ge(rsum_done, NQ * a + n + 1)
                nc.vector.tensor_tensor(p, p, rtotal[:, n, :].unsqueeze(2).broadcast_to([P, H, TK]), ALU.mult)\
                    .then_inc(probs_ready, 1)

            def one_pass(f, a, nxt):
                for step, n in steps(True, a is not None, nxt) if f is not None else FIRST:
                    if step == "COUNT":
                        dve.wait_ge(checked, NP)
                        nc.vector.tensor_reduce(inexact_row[:], inexact[:], AX_X, ALU.add).then_inc(row_summed, 1)
                        dve.wait_ge(flag_summed, 1)
                        nc.vector.tensor_copy(flag[:], fb[0:1, 0, 0:1]).then_inc(flag_ready, 1)
                    if step == "CHECK":
                        dve.wait_ge(rounded, n + 1)
                        nc.vector.scalar_tensor_tensor(out=stage[n % STAGES][:], in0=stage[n % STAGES][:], scalar=1.0,
                                                       in1=pieces[n][1].bitcast(F32), op0=ALU.mult, op1=ALU.not_equal,
                                                       accum_out=inexact[:, n:n + 1]).then_inc(checked, 1)
                    if step == "L1":
                        dve.wait_ge(up_ready, KH * f + n + 1)
                        dve.wait_ge(silu_done, KH * f + n + 1)
                        nc.vector.scalar_tensor_tensor(out=a_f32[:, n, :], in0=fb[:, 2 * (n % 2) + 1, :], scalar=s2_sb[:, n:n + 1],
                                                       in1=a_f32[:, n, :], op0=ALU.mult, op1=ALU.mult).then_inc(up_used, 1)
                    if (step == "L1" and n > 0) or step == "L1E":
                        m = n - 1 if step == "L1" else KH - 1
                        dve.wait_ge(h1_hi_done, KH * f + m + 1)
                        nc.vector.tensor_tensor(a_lo[:, m, :], a_f32[:, m, :], a_hi[:, m, :].bitcast(F32), ALU.subtract)\
                            .then_inc(h1_done, 1)
                    if step in ("L2", "L3"):
                        f32, hi, lo, ready, done = ((b_f32, b_hi, b_lo, gelu2_done, h2_done) if step == "L2"
                                                    else (a_f32, a_hi, a_lo, gelu3_done, h3_done))
                        dve.wait_ge(ready, KH * f + n + 1)
                        nc.vector.tensor_tensor(lo[:, n, :], f32[:, n, :], hi[:, n, :].bitcast(F32), ALU.subtract).then_inc(done, 1)
                    if step == "L4":
                        dve.wait_ge(l4_ready, 2 * f + n + 1)
                        if n == 0:
                            dve.wait_ge(stored, 16 * f + 16)
                        nc.vector.tensor_tensor(out_sb[:, 2 * n:2 * n + 2, :],
                                                fb[:, 2 + n, :].rearrange("p (j d) -> p j d", j=2),
                                                s3_sb.unsqueeze(1).broadcast_to([P, 2, D]), ALU.mult).then_inc(out_scaled, 1)
                    if step == "KV":
                        dve.wait_ge(v_ready, a + 1)
                        nc.vector.tensor_tensor(v_sb[:], ab[0:TK, 3, :].rearrange("p (b d) -> p b d", b=NB),
                                                bv_sb[0:TK].unsqueeze(1).broadcast_to([TK, NB, D]), ALU.add).then_inc(v_done, 1)
                    if step == "S":
                        pair = 2 if n % 2 == 0 else 0
                        scores = ab[:, pair:pair + 2, 0:G4].rearrange("p g (h c) -> p g h c", h=4)
                        dve.wait_ge(s_ready, NQ * a + n + 1)
                        m = mx[:, n, :].rearrange("p (g h) -> p g h", g=HG)
                        p = probs[:, n, :].rearrange("p (g h c) -> p g h c", g=HG, h=4)
                        if n == 2 and not (isinstance(a, int) and a == 0):
                            dve.wait_ge(x1_kept, a)
                        if n % (TQ // P) == 0:
                            nc.vector.tensor_tensor(p, scores, mask[:].unsqueeze(1).unsqueeze(1).broadcast_to([P, HG, 4, TK]),
                                                    ALU.add).then_inc(masked, 1)
                            dve.wait_ge(masked, NB * a + n // 2 + 1)
                            scores = p
                        nc.vector.tensor_reduce(m, scores, AX_X, ALU.max).then_inc(max_done, 1)
                        dve.wait_ge(max_done, NQ * a + n + 1)
                        nc.vector.tensor_tensor(p, scores, m.unsqueeze(3).broadcast_to([P, HG, 4, TK]), ALU.subtract)\
                            .then_inc(shifted, 1)
                    if step == "EXP":
                        soften(n, a)
                    if step == "PT":
                        dve.wait_ge(pt_ready, NQ * a + n + 1)
                        q0 = (n % 2) * P
                        nc.vector.tensor_copy(attn_t[:, 4:8, q0:q0 + P],
                                              ab[0:TK, (2, 0, 0, 2)[n] + 1, :].rearrange("p (h q) -> p h q", h=4))\
                            .then_inc(pt_dve_done, 1)
                    if step == "O":
                        dve.wait_ge(o_ready, a + 1)
                        dve.wait_ge(x1_seeded, a + 1)
                        nc.vector.tensor_tensor(x1[:], ab[:, 2:4, :].rearrange("p c (j d) -> p (c j) d", d=D), x1[:], ALU.add)\
                            .then_inc(x1_done, 1)
                    if step == "LN2S":
                        dve.wait_ge(x1_done, a + 1)
                        ln_stats_of(x1, 1, a)
                    if step == "LN2A":
                        ln_apply(x1, 1, a)
                    if step == "T2":
                        dve.wait_ge(ln2hi_done, a + 1)
                        nc.vector.tensor_tensor(ln2_lo[:], ab[:, 0:2, :], ln2_hi[:].bitcast(F32), ALU.subtract).then_inc(ln2t_done, 1)
                    if step == "LN1S":
                        dve.wait_ge(x_loaded, 16 * (a + 2))
                        ln_stats_of(x_in, 0, a + 1)
                    if step == "LN1A":
                        ln_apply(x_in, 0, a + 1)

            nc.vector.memset(ones[:], 1.0).then_inc(out_scaled, 2)
            nc.vector.memset(eps[:], EPS)
            nc.vector.memset(minus_half[:], -0.5).then_inc(dve_consts, 1)
            nc.vector.memset(flag[:], 0).then_inc(ring_used, 2)
            nc.vector.memset(inexact_row[:], 0.0).then_inc(stored, 16)
            nc.vector.memset(k_diag[:], 0.0).then_inc(kdiag_zero, 1)
            dve.wait_ge(x_loaded, 16)
            ln_stats_of(x_in, 0, 0)
            ln_apply(x_in, 0, 0)
            dve.wait_ge(vec_loaded, 16)
            dve.wait_ge(out_ready, 2)
            one_pass(None, 0, True)
            whole_program(dve, one_pass)

        @block.gpsimd
        def _(pool):
            def rstd_of(i, a):
                pool.wait_ge(ln_mv[i], a + 1)
                nc.gpsimd.tensor_tensor(veps[i][:], mv[i][:, :, 1], eps[:], ALU.add).then_inc(ln_veps[i], 1)
                pool.wait_ge(ln_veps[i], a + 1)
                nc.gpsimd.tensor_tensor(rstd[i][:], veps[i][:], minus_half[:], ALU.pow).then_inc(ln_rstd[i], 1)

            def one_pass(f, a, nxt):
                for step, n in steps(True, a is not None, nxt) if f is not None else FIRST:
                    if step == "SEED":
                        pool.wait_ge(pt_ready, NQ * a + NQ)
                        if not (isinstance(a, int) and a == 0):
                            pool.wait_ge(x1_kept, a)
                        nc.gpsimd.tensor_tensor(x1[:], x_in[:], bo_sb.unsqueeze(1).broadcast_to([P, NQ, D]), ALU.add)\
                            .then_inc(x1_seeded, 1)
                    if step == "LN2S":
                        rstd_of(1, a)
                    if step == "LN1S":
                        rstd_of(0, a + 1)
                    if step == "L4":
                        half = slice(2 * n, 2 * n + 2)
                        pool.wait_ge(out_scaled, 2 * f + n + 3)
                        if n == 0:
                            pool.wait_ge(x1_kept, f + 1)
                        nc.gpsimd.tensor_tensor(out_sb[:, half, :], out_sb[:, half, :], x1_keep[:, half, :], ALU.add)\
                            .then_inc(out_ready, 1)

            nc.gpsimd.memset(id32[:], 0.0).then_inc(const_set, 1)
            nc.gpsimd.memset(mask[:], 0.0).then_inc(const_set, 1)
            pool.wait_ge(const_set, 2)
            nc.gpsimd.affine_select(out=id32[:], in_=id32[:], compare_op=ALU.not_equal, fill=1.0, base=0,
                                    pattern=[[-1, P]], channel_multiplier=1).then_inc(id_ready, 1)
            nc.gpsimd.affine_select(out=mask[:], in_=mask[:], compare_op=ALU.is_ge, fill=MASKED, base=0,
                                    pattern=[[-1, TK]], channel_multiplier=1).then_inc(out_ready, 2)
            pool.wait_ge(dve_consts, 1)
            rstd_of(0, 0)
            pool.wait_ge(vec_loaded, 16)
            one_pass(None, 0, True)
            whole_program(pool, one_pass)


def kernel(**inputs):
    import numpy as np
    import concourse.bacc as bacc
    from concourse import mybir as mb
    from concourse.bass_utils import run_bass_kernel_spmd

    def rows(name):
        w = np.asarray(inputs[name]).T
        return np.ascontiguousarray(w.reshape(-1, P, w.shape[1]).transpose(1, 0, 2))

    def per_feature(name):
        return np.asarray(inputs[name]).reshape(-1, P).T

    def over_rows(name):
        v = np.asarray(inputs[name])
        return np.broadcast_to(v, (P, v.shape[0]))

    ctx = np.asarray(inputs["ctx_1024"]).reshape(NT, NB * TK, KD, P)
    arrays = {
        "x": np.ascontiguousarray(np.asarray(inputs["x"]).reshape(B * TQ, D)),
        "ctx_t": np.ascontiguousarray(ctx.transpose(0, 3, 2, 1)),
        "w_att": np.ascontiguousarray(np.stack([rows("L0_xattn_" + n) for n in ("Wq", "Wk", "Wv", "Wo")], axis=1)),
        "vectors": np.ascontiguousarray(np.concatenate(
            [per_feature("L0_ffn_" + n) for n in ("w1_s", "w2_s", "h1_s", "h2_s")]
            + [per_feature("L0_xattn_" + n) for n in ("bq", "bk")]
            + [over_rows("L0_xattn_" + n) for n in ("bo", "bv")] + [over_rows("L0_ffn_w3_s")], axis=1)),
        "w1": rows("L0_ffn_w1_w"), "w2": rows("L0_ffn_w2_w"), "h1": rows("L0_ffn_h1_w"),
        "h2": rows("L0_ffn_h2_w"), "w3": rows("L0_ffn_w3_w"),
    }
    nc = bacc.Bacc("TRN2", target_bir_lowering=False, num_devices=1)
    dram = {f"in_{k}": v for k, v in arrays.items()}
    args = {k: nc.dram_tensor(f"in_{k}", v.shape, mb.dt.from_np(v.dtype), kind="ExternalInput").ap() for k, v in arrays.items()}
    out = nc.dram_tensor("out_0", (B * TQ, D), mb.dt.float32, kind="ExternalOutput").ap()
    build_kernel(nc, **args, out=out)
    result = run_bass_kernel_spmd(nc, [dram], core_ids=[0])
    return result.results[0]["out_0"].reshape(B, TQ, D)
```
